# Optimizing a Trainium2 kernel written in Bass

```python
import numpy as np
import jax
import jax.numpy as jnp

def _softmax(x, axis=-1):
    return jax.nn.softmax(x, axis=axis)

def _gelu(x):
    return jax.nn.gelu(x, approximate=True)

def _silu(x):
    return jax.nn.silu(x)

def _sigmoid(x):
    return jax.nn.sigmoid(x)

def _layernorm(x, axis=-1, eps=1e-05):
    m = jnp.mean(x, axis=axis, keepdims=True)
    v = jnp.var(x, axis=axis, keepdims=True)
    return (x - m) / jnp.sqrt(v + eps)

def _scatter_add(tgt, idx, src, axis=0):
    return tgt.at[idx].add(src)

def _segment_sum(src, seg, n):
    return jax.ops.segment_sum(src, seg, n)
kernel_name = 'mk_macaron_d1_jaxref_r4_948a5a'

def setup_inputs(seed: int=0):
    np.random.seed(seed)
    _w = jnp.asarray

    def _L0_attn_setup():
        import jax, jax.numpy as jnp
        import numpy as np
        B, T, D, K = (4, 512, 512, 4)
        LN_EPS = 1e-05

        def _gated_scan(lam, z):
            b, t, d = z.shape
            k = lam.shape[0]
            a = jnp.broadcast_to(lam.astype(z.dtype), (b, t, d, k))
            zb = jnp.broadcast_to(z[..., None], (b, t, d, k))

            def combine(c1, c2):
                a1, b1 = c1
                a2, b2 = c2
                return (a1 * a2, b2 + a2 * b1)
            _, m = jax.lax.associative_scan(combine, (a, zb), axis=1)
            return m
        key = jax.random.key(seed)
        k_x, k_w = jax.random.split(key, 2)
        x = jax.random.normal(k_x, (B, T, D), dtype=jnp.float32)
        W = jax.random.normal(k_w, (D, D), dtype=jnp.float32) / np.sqrt(D)
        lam0 = jnp.asarray([0.999, 0.99, 0.9, 0.999], dtype=jnp.float32)
        lam_logit = jnp.log(lam0 / (1.0 - lam0))
        eta = jnp.asarray([1.0, 1.0, 1.0, 0.1], dtype=jnp.float32)
        gamma = jnp.ones((D,), dtype=jnp.float32)
        beta = jnp.zeros((D,), dtype=jnp.float32)
        return {'x': x, 'W': W, 'lam_logit': lam_logit, 'eta': eta, 'gamma': gamma, 'beta': beta}
    _L0_attn_in = _L0_attn_setup()

    def _L0_ffn_setup():
        import jax, jax.numpy as jnp
        import numpy as np
        DIM_IN = 512
        DIM_HIDDEN = 2048
        key = jax.random.key(seed)
        k_x, k_g, k_u, k_d = jax.random.split(key, 4)
        s_in = 1.0 / np.sqrt(DIM_IN)
        s_hid = 1.0 / np.sqrt(DIM_HIDDEN)
        x = jax.random.normal(k_x, (4, 512, DIM_IN), dtype=jnp.float32)
        w_gate = jax.random.uniform(k_g, (DIM_HIDDEN, DIM_IN), jnp.float32, -s_in, s_in)
        w_up = jax.random.uniform(k_u, (DIM_HIDDEN, DIM_IN), jnp.float32, -s_in, s_in)
        w_down = jax.random.uniform(k_d, (DIM_IN, DIM_HIDDEN), jnp.float32, -s_hid, s_hid)
        return {'x': x, 'w_gate': w_gate, 'w_up': w_up, 'w_down': w_down}
    _L0_ffn_in = _L0_ffn_setup()
    _d = {'L0_attn_x': _L0_attn_in['x'], 'L0_attn_W': _L0_attn_in['W'], 'L0_attn_lam_logit': _L0_attn_in['lam_logit'], 'L0_attn_eta': _L0_attn_in['eta'], 'L0_attn_gamma': _L0_attn_in['gamma'], 'L0_attn_beta': _L0_attn_in['beta'], 'L0_ffn_w_gate': _L0_ffn_in['w_gate'], 'L0_ffn_w_up': _L0_ffn_in['w_up'], 'L0_ffn_w_down': _L0_ffn_in['w_down']}
    _x0 = _d['L0_attn_x']
    _d['L0_attn_x'] = jax.random.normal(jax.random.fold_in(jax.random.key(seed), 1), (4, 512, 512), dtype=_x0.dtype)
    del _x0
    return _d

def reference(L0_attn_x, L0_attn_W, L0_attn_lam_logit, L0_attn_eta, L0_attn_gamma, L0_attn_beta, L0_ffn_w_gate, L0_ffn_w_up, L0_ffn_w_down):

    def _L0_attn_ref(x, W, lam_logit, eta, gamma, beta):
        import jax, jax.numpy as jnp
        import numpy as np
        B, T, D, K = (4, 512, 512, 4)
        LN_EPS = 1e-05

        def _gated_scan(lam, z):
            b, t, d = z.shape
            k = lam.shape[0]
            a = jnp.broadcast_to(lam.astype(z.dtype), (b, t, d, k))
            zb = jnp.broadcast_to(z[..., None], (b, t, d, k))

            def combine(c1, c2):
                a1, b1 = c1
                a2, b2 = c2
                return (a1 * a2, b2 + a2 * b1)
            _, m = jax.lax.associative_scan(combine, (a, zb), axis=1)
            return m
        lam = jax.nn.sigmoid(lam_logit)
        z = jnp.einsum('btd,ed->bte', x, W)
        m = _gated_scan(lam, z)
        h = z + jnp.einsum('btdk,k->btd', m, eta)
        mu = jnp.mean(h, axis=-1, keepdims=True)
        var = jnp.mean(jnp.square(h - mu), axis=-1, keepdims=True)
        return gamma * (h - mu) * jax.lax.rsqrt(var + LN_EPS) + beta

    def _L0_ffn_ref(x, w_gate, w_up, w_down):
        import jax, jax.numpy as jnp
        import numpy as np
        DIM_IN = 512
        DIM_HIDDEN = 2048
        gate = jnp.einsum('bsd,hd->bsh', x, w_gate)
        up = jnp.einsum('bsd,hd->bsh', x, w_up)
        gated = jax.nn.silu(gate) * up
        return jnp.einsum('bsh,dh->bsd', gated, w_down)
    x = L0_attn_x
    x = x + 0.5 * _L0_ffn_ref(_layernorm(x, axis=-1), L0_ffn_w_gate, L0_ffn_w_up, L0_ffn_w_down)
    x = x + _L0_attn_ref(_layernorm(x, axis=-1), L0_attn_W, L0_attn_lam_logit, L0_attn_eta, L0_attn_gamma, L0_attn_beta)
    x = x + 0.5 * _L0_ffn_ref(_layernorm(x, axis=-1), L0_ffn_w_gate, L0_ffn_w_up, L0_ffn_w_down)
    return x

_drawn_inputs = setup_inputs


def setup_inputs(seed=0):
    import zlib

    import numpy as np

    out = dict(_drawn_inputs(seed))
    spreads = {'L0_attn_gamma': (1.0, 0.2), 'L0_attn_beta': (0.0, 0.1)}
    factors = {}
    for name, (base, spread) in spreads.items():
        noise = np.random.default_rng([zlib.crc32(name.encode()), seed]).standard_normal(out[name].shape)
        drawn = base * np.exp(spread * noise) if base else spread * noise
        out[name] = jnp.asarray(drawn.astype(out[name].dtype))
    for name, factor in factors.items():
        out[name] = (out[name] * factor).astype(out[name].dtype)
    return out
```

```python
from collections import namedtuple
from contextlib import ExitStack

import concourse.bass as bass
from concourse import mybir

F32 = mybir.dt.float32
F32R = mybir.dt.float32r
ALU = mybir.AluOpType
ACT = mybir.ActivationFunctionType

P = 128
EPS = 1e-5

Step = namedtuple("Step", "p odd t tp beside s sp tile f0 f done last")


def macaron_kernel(nc, x_in, w_ffn_in, w_scan_in, lam_logit_in, eta_in, gamma_in, beta_in, out):
    tiles, tokens, D = x_in.shape
    H = w_ffn_in.shape[0] * P
    K = lam_logit_in.shape[0]
    DT = D // P
    ST = tokens // P
    HT = H // P
    GU = 2 * DT * P
    LAST = HT - 1
    passes = 2 * tiles
    PRE, SCAN, POST = 2, 6, 11
    assert tokens == 512 and D == 512 and DT == ST == 4 and HT == 16 and tiles == 4 and K == 4

    with ExitStack() as ctx:
        def sb(name, shape, dt=F32):
            return ctx.enter_context(nc.sbuf_tensor(name, shape, dt))

        def sem(name):
            return ctx.enter_context(nc.semaphore(name))

        w_ffn = sb("w_ffn", [P, HT, GU + D])
        w_scan = sb("w_scan", [P, DT * P])
        w_scan_hi = sb("w_scan_hi", [P, DT * P], F32R)
        w_scan_lo = sb("w_scan_lo", [P, DT * P], F32R)
        gu_hi = sb("gu_hi", [P, 2, GU], F32R)
        gu_lo = sb("gu_lo", [P, 2, GU], F32R)
        dn_hi = sb("dn_hi", [P, 2, D], F32R)
        dn_lo = sb("dn_lo", [P, 2, D], F32R)
        xt_hi = sb("xt_hi", [P, 2, DT, tokens], F32R)
        xt_lo = sb("xt_lo", [P, 2, DT, tokens], F32R)
        hid = sb("hid", [P, 2, tokens])
        hid_hi = sb("hid_hi", [P, 2, tokens], F32R)
        hid_lo = sb("hid_lo", [P, 2, tokens], F32R)
        x_tok = sb("x_tok", [P, tiles * ST, D])
        rows = sb("rows", [P, 2, D])
        scan_sum = sb("scan_sum", [P, DT, tokens])
        gamma = sb("gamma", [P, D])
        beta = sb("beta", [P, D])
        ident = sb("ident", [P, P])
        lam = sb("lam", [P, K])
        lam_tmp = sb("lam_tmp", [P, 2, K])
        eta = sb("eta", [P, K])
        minus_half = sb("minus_half", [P, 1])
        ln_stats = sb("ln_stats", [P, 6])
        ln_mv = sb("ln_mv", [P, 2])
        ln_ve = sb("ln_ve", [P, 1])
        ln_rstd = sb("ln_rstd", [P, 1])
        post_stats = sb("post_stats", [P, 6])
        post_mv = sb("post_mv", [P, 2])
        post_ve = sb("post_ve", [P, 1])
        post_rstd = sb("post_rstd", [P, 1])

        def bank(name):
            return ctx.enter_context(nc.psum_tensor(name, [P, 512], F32))

        gate_ps = bank("gate_ps")
        up_ps = bank("up_ps")
        down_ps = [bank(f"down_ps{q}") for q in range(ST)]
        aux_ps = [bank(f"aux_ps{q}") for q in range(2)]

        w_arrived = [sem(f"w_arrived{t}") for t in range(HT)]
        x0_arrived = [sem(f"x0_arrived{s}") for s in range(ST)]
        x_arrived = [sem(f"x_arrived{b}") for b in range(tiles)]
        lam_arrived = sem("lam_arrived")
        rows_arrived = sem("rows_arrived")
        w_scan_arrived = sem("w_scan_arrived")
        stored = sem("stored")
        ident_zero = sem("ident_zero")
        ident_ready = sem("ident_ready")
        exp_done = sem("exp_done")
        lam_steps = sem("lam_steps")
        gu_hi_ready = sem("gu_hi_ready")
        gu_lo_ready = sem("gu_lo_ready")
        dn_hi_ready = sem("dn_hi_ready")
        dn_lo_ready = sem("dn_lo_ready")
        gate_done = sem("gate_done")
        up_done = sem("up_done")
        down_done = sem("down_done")
        silu_done = sem("silu_done")
        hid_done = sem("hid_done")
        hid_hi_ready = sem("hid_hi_ready")
        hid_lo_ready = sem("hid_lo_ready")
        y_added = sem("y_added")
        ln_mv_done = sem("ln_mv_done")
        ln_ve_done = sem("ln_ve_done")
        ln_rstd_done = sem("ln_rstd_done")
        row_ready = sem("row_ready")
        turned = sem("turned")
        xt_hi_ready = sem("xt_hi_ready")
        xt_lo_ready = sem("xt_lo_ready")
        w_scan_hi_ready = sem("w_scan_hi_ready")
        w_scan_lo_ready = sem("w_scan_lo_ready")
        z_done = sem("z_done")
        z_bank_free = sem("z_bank_free")
        scan_steps = sem("scan_steps")
        scan_sum_ready = sem("scan_sum_ready")
        turned_back = sem("turned_back")
        post_mv_done = sem("post_mv_done")
        post_ve_done = sem("post_ve_done")
        post_rstd_done = sem("post_rstd_done")
        post_steps = sem("post_steps")

        def wait(eng, semaphore, n):
            if isinstance(n, int) and n <= 0:
                return
            eng.wait_ge(semaphore, n)

        def walk(eng, step, unroll_first=False, unroll_post=False):
            def run(t, count, beside, p, odd, tile, f, done, last=False, unroll=False):
                def pair(t, s, tp, n):
                    for u in range(n):
                        step(Step(p, odd, t + u, (tp + u) % 2, beside, s + u, u % 2, tile, f,
                                  f + s + u, done, last))
                if count <= 2 or unroll:
                    for s in range(0, count, 2):
                        pair(t + s, s, t % 2, min(2, count - s))
                else:
                    with eng.Fori(0, count // 2) as k:
                        pair(2 * k + t, 2 * k, t % 2, 2)

            def one_pass(p, odd, kind, tile, f, done, final=False):
                plain = dict(p=p, odd=odd, tile=tile, f=f, done=done)
                first = dict(plain, unroll=unroll_first and isinstance(p, int) and p == 0)
                if kind == "scan":
                    run(0, PRE, "", **first)
                    run(PRE, ST, "pre", **plain)
                    run(SCAN, DT, "scan", **plain)
                    run(SCAN + DT, POST - SCAN - DT, "", **plain)
                    run(POST, ST, "post", p, odd, tile, f + ST, done, unroll=unroll_post)
                    run(LAST, 1, "", last=final, **plain)
                else:
                    run(0, PRE, "", **first)
                    if kind == "ln":
                        run(PRE, ST, "ln", **first)
                        run(PRE + ST, LAST - 1 - PRE - ST, "", **first)
                    else:
                        run(PRE, LAST - 1 - PRE, "", **first)
                    run(LAST - 1, 1, "", **plain)
                    run(LAST, 1, "", last=final, **plain)

            one_pass(0, 0, "ln", 1, ST, None)
            one_pass(1, 1, "scan", 0, 2 * ST, 0)
            with eng.Fori(1, tiles - 1) as i:
                one_pass(2 * i, 0, "ln", i + 1, 12 * i + 4, i)
                one_pass(2 * i + 1, 1, "scan", i, 12 * i + 8, i - 1)
            one_pass(passes - 2, 0, "scan", tiles - 1, 12 * (tiles - 1) + 4, tiles - 1)
            one_pass(passes - 1, 1, "", None, 12 * tiles, tiles - 2, final=True)

        block = ctx.enter_context(nc.Block())

        @block.sync
        def _(sp):
            x_v = x_in.rearrange("b (s p) d -> b p s d", p=P)
            out_v = out.rearrange("b (s p) d -> b p s d", p=P)

            def load_w(t):
                sp.dma_start(w_ffn[:, t, :], w_ffn_in[t]).then_inc(w_arrived[t], 16)

            def load_x(b):
                sp.dma_start(x_tok[:, b * ST:(b + 1) * ST, :], x_v[b]).then_inc(x_arrived[b], 16)

            def load_w_scan(tile, j):
                wait(sp, w_scan_lo_ready, tile * DT + j)
                sp.dma_start(w_scan[:, :], w_scan_in[j]).then_inc(w_scan_arrived, 16)

            def store(b, p):
                sp.wait_ge(y_added, (p + 1) * ST)
                sp.dma_start(out_v[b], x_tok[:, bass.ds(b * ST, ST), :]).then_inc(stored, 16)

            sp.dma_start(x_tok[:, 0, :], x_v[0, :, 0, :]).then_inc(x0_arrived[0], 16)
            load_w(0)
            for s in range(1, ST):
                sp.dma_start(x_tok[:, s, :], x_v[0, :, s, :]).then_inc(x0_arrived[s], 16)
            load_w(1)
            load_w(2)
            load_x(1)
            for t in range(3, HT):
                load_w(t)
            for b in range(2, tiles):
                load_x(b)
            for j in range(DT):
                load_w_scan(0, j)
            with sp.Fori(1, tiles - 1) as i:
                store(i - 1, 2 * i)
                with sp.Fori(0, DT) as j:
                    load_w_scan(i, j)
            for j in range(DT):
                load_w_scan(tiles - 1, j)
            store(tiles - 2, passes - 2)
            store(tiles - 1, passes - 1)
            sp.wait_ge(stored, 16 * (tiles - 1) + 16)

        @block.scalar
        def _(act):
            def split_gu(p, t, slot, g):
                if isinstance(p, int) and p == 0:
                    act.wait_ge(w_arrived[t], 16)
                wait(act, up_done, g - 1)
                act.copy(gu_hi[:, slot, :], w_ffn[:, t, 0:GU]).then_inc(gu_hi_ready, 1)

            def split_xt(f, slot, s):
                act.wait_ge(turned, f + 1)
                act.copy(xt_hi[:, slot, :, bass.ds(s * P, P)],
                         aux_ps[1][:, :].rearrange("p (c n) -> p c n", c=DT)).then_inc(xt_hi_ready, 1)

            def step(c):
                g = c.p * HT + c.t
                if not c.last:
                    last = isinstance(c.t, int) and c.t == LAST
                    if last:
                        split_gu(c.p + 1, 0, (c.tp + 1) % 2, g + 1)
                    else:
                        split_gu(c.p, c.t + 1, (c.tp + 1) % 2, g + 1)
                wait(act, down_done, g - 1)
                act.copy(dn_hi[:, c.tp, :], w_ffn[:, c.t, GU:GU + D]).then_inc(dn_hi_ready, 1)
                act.wait_ge(gate_done, g + 1)
                wait(act, hid_lo_ready, g - 1)
                act.activation(hid[:, c.tp, :], gate_ps[:, :], ACT.Silu).then_inc(silu_done, 1)
                if c.beside == "scan":
                    act.wait_ge(w_scan_arrived, (c.tile * DT + c.s) * 16 + 16)
                    act.copy(w_scan_hi[:, :], w_scan[:, :]).then_inc(w_scan_hi_ready, 1)
                act.wait_ge(hid_done, g + 1)
                wait(act, down_done, g - 1)
                act.copy(hid_hi[:, c.tp, :], hid[:, c.tp, :]).then_inc(hid_hi_ready, 1)
                if c.beside in ("ln", "pre", "post"):
                    split_xt(c.f, 1 - c.odd, c.s)

            act.dma_start(lam_tmp[:, 0, :], lam_logit_in.rearrange("(o k) -> o k", o=1).to_broadcast([P, K])
                          ).then_inc(lam_arrived, 16)
            act.dma_start(eta[:, :], eta_in.rearrange("(o k) -> o k", o=1).to_broadcast([P, K])
                          ).then_inc(rows_arrived, 16)
            act.dma_start(gamma[:, :], gamma_in.rearrange("(o d) -> o d", o=1).to_broadcast([P, D])
                          ).then_inc(rows_arrived, 16)
            act.dma_start(beta[:, :], beta_in.rearrange("(o d) -> o d", o=1).to_broadcast([P, D])
                          ).then_inc(rows_arrived, 16)
            act.wait_ge(lam_arrived, 16)
            act.activation(lam_tmp[:, 1, :], lam_tmp[:, 0, :], ACT.Exp, scale=-1.0).then_inc(exp_done, 1)
            for s in range(ST - 1):
                split_xt(s, 0, s)
            split_gu(0, 0, 0, 0)
            split_xt(ST - 1, 0, ST - 1)
            walk(act, step, unroll_first=True)

        @block.gpsimd
        def _(pool):
            def ln(f):
                pool.wait_ge(ln_ve_done, f + 1)
                pool.tensor_tensor(ln_rstd[:, :], ln_ve[:, :], minus_half[:, :], ALU.pow).then_inc(ln_rstd_done, 1)

            def post_norm(n):
                pool.wait_ge(post_ve_done, n + 1)
                pool.tensor_tensor(post_rstd[:, :], post_ve[:, :], minus_half[:, :], ALU.pow
                                   ).then_inc(post_rstd_done, 1)

            def split_gu(t, slot, g):
                pool.wait_ge(gu_hi_ready, g + 1)
                pool.tensor_tensor(gu_lo[:, slot, :], w_ffn[:, t, 0:GU], gu_hi[:, slot, :].bitcast(F32),
                                   ALU.subtract).then_inc(gu_lo_ready, 1)

            def step(c):
                g = c.p * HT + c.t
                if c.beside in ("ln", "pre"):
                    ln(c.f)
                if c.beside == "post":
                    post_norm(c.tile * ST + c.s)
                if not c.last:
                    last = isinstance(c.t, int) and c.t == LAST
                    split_gu(0 if last else c.t + 1, (c.tp + 1) % 2, g + 1)
                if c.beside == "post":
                    ln(c.f)
                pool.wait_ge(dn_hi_ready, g + 1)
                pool.tensor_tensor(dn_lo[:, c.tp, :], w_ffn[:, c.t, GU:GU + D], dn_hi[:, c.tp, :].bitcast(F32),
                                   ALU.subtract).then_inc(dn_lo_ready, 1)
                if c.beside == "scan":
                    pool.wait_ge(w_scan_hi_ready, c.tile * DT + c.s + 1)
                    pool.tensor_tensor(w_scan_lo[:, :], w_scan[:, :], w_scan_hi[:, :].bitcast(F32),
                                       ALU.subtract).then_inc(w_scan_lo_ready, 1)

            pool.memset(ident[:, :], 0.0).then_inc(ident_zero, 1)
            pool.memset(minus_half[:, :], -0.5).then_inc(ident_zero, 1)
            pool.wait_ge(ident_zero, 2)
            pool.affine_select(out=ident[:, :], in_=ident[:, :], compare_op=ALU.not_equal, fill=1.0, base=0,
                               pattern=[[-1, P]], channel_multiplier=1).then_inc(ident_ready, 1)
            for f in range(ST):
                ln(f)
            split_gu(0, 0, 0)
            walk(pool, step)

        @block.vector
        def _(dve):
            def ln(f, sp, x):
                dve.bn_stats(ln_stats[:, :], x)
                dve.drain()
                dve.bn_aggr(ln_mv[:, :], ln_stats[:, :]).then_inc(ln_mv_done, 1)
                dve.wait_ge(ln_mv_done, f + 1)
                dve.tensor_scalar(ln_ve[:, :], ln_mv[:, 1:2], EPS, None, ALU.add).then_inc(ln_ve_done, 1)
                wait(dve, turned, f - 1)
                dve.wait_ge(ln_rstd_done, f + 1)
                dve.tensor_scalar(rows[:, sp, :], x, ln_mv[:, 0:1], ln_rstd[:, 0:1], ALU.subtract,
                                  ALU.mult).then_inc(row_ready, 1)

            def split_xt(f, slot, s):
                dve.wait_ge(xt_hi_ready, f + 1)
                dst = bass.ds(s * P, P)
                dve.tensor_tensor(xt_lo[:, slot, :, dst], aux_ps[1][:, :].rearrange("p (c n) -> p c n", c=DT),
                                  xt_hi[:, slot, :, dst].bitcast(F32), ALU.subtract).then_inc(xt_lo_ready, 1)

            def scan(c):
                n = c.tile * DT + c.s
                z = aux_ps[c.sp][:, :]
                total = scan_sum[:, c.s, :]

                def m(k):
                    return dve.tensor_tensor_scan(rows[:, k % 2, :], lam[:, k:k + 1].to_broadcast([P, tokens]),
                                                  z, 0.0, ALU.mult, ALU.add)

                def add(k, to):
                    return dve.scalar_tensor_tensor(total, rows[:, k % 2, :], eta[:, k:k + 1], to, ALU.mult,
                                                    ALU.add)

                dve.drain()
                dve.wait_ge(z_done, n + 1)
                m(0).then_inc(scan_steps, 1)
                m(1).then_inc(scan_steps, 1)
                dve.wait_ge(scan_steps, n * 6 + 1)
                add(0, z).then_inc(scan_steps, 1)
                dve.wait_ge(scan_steps, n * 6 + 3)
                m(2).then_inc(scan_steps, 1)
                add(1, total).then_inc(scan_steps, 1)
                dve.wait_ge(scan_steps, n * 6 + 5)
                m(3).then_inc(z_bank_free, 1)
                add(2, total).then_inc(scan_steps, 1)
                dve.wait_ge(z_bank_free, n + 3)
                dve.wait_ge(scan_steps, n * 6 + 6)
                add(3, total).then_inc(scan_sum_ready, 1)

            def post(c):
                n = c.tile * ST + c.s
                x = x_tok[:, c.tile * ST + c.s, :]
                dve.wait_ge(turned_back, n + 1)
                dve.bn_stats(post_stats[:, :], aux_ps[0][:, :])
                dve.drain()
                dve.bn_aggr(post_mv[:, :], post_stats[:, :]).then_inc(post_mv_done, 1)
                dve.wait_ge(post_mv_done, n + 1)
                dve.tensor_scalar(post_ve[:, :], post_mv[:, 1:2], EPS, None, ALU.add).then_inc(post_ve_done, 1)
                dve.wait_ge(turned, c.f - 1)
                dve.scalar_tensor_tensor(rows[:, c.sp, :], aux_ps[0][:, :], post_mv[:, 0:1], gamma[:, :],
                                         ALU.subtract, ALU.mult).then_inc(post_steps, 1)
                dve.wait_ge(post_steps, n * 3 + 1)
                dve.wait_ge(post_rstd_done, n + 1)
                dve.scalar_tensor_tensor(rows[:, c.sp, :], rows[:, c.sp, :], post_rstd[:, 0:1], beta[:, :],
                                         ALU.mult, ALU.add).then_inc(post_steps, 1)
                dve.wait_ge(post_steps, n * 3 + 2)
                dve.tensor_tensor(x, x, rows[:, c.sp, :], ALU.add).then_inc(post_steps, 1)

            def add_y(p, b):
                dve.wait_ge(down_done, (p + 1) * HT)
                for q in range(ST):
                    x = x_tok[:, b * ST + q, :]
                    dve.scalar_tensor_tensor(x, down_ps[q][:, :], 0.5, x, ALU.mult, ALU.add).then_inc(y_added, 1)

            def step(c):
                g = c.p * HT + c.t
                if c.beside == "ln":
                    for b in (1,) if isinstance(c.p, int) and c.p == 0 else range(2, tiles):
                        dve.wait_ge(x_arrived[b], 16)
                if c.beside == "post":
                    post(c)
                if c.beside in ("pre", "post"):
                    dve.drain()
                if c.beside in ("ln", "pre", "post"):
                    ln(c.f, c.sp, x_tok[:, c.tile * ST + c.s, :])
                dve.wait_ge(silu_done, g + 1)
                dve.wait_ge(up_done, g + 1)
                dve.tensor_tensor(hid[:, c.tp, :], hid[:, c.tp, :], up_ps[:, :], ALU.mult).then_inc(hid_done, 1)
                dve.wait_ge(hid_hi_ready, g + 1)
                wait(dve, down_done, g - 1)
                dve.tensor_tensor(hid_lo[:, c.tp, :], hid[:, c.tp, :], hid_hi[:, c.tp, :].bitcast(F32),
                                  ALU.subtract).then_inc(hid_lo_ready, 1)
                if isinstance(c.t, int) and c.t == 0 and c.done is not None:
                    add_y(c.p - 1, c.done)
                if c.beside in ("ln", "pre", "post"):
                    split_xt(c.f, 1 - c.odd, c.s)
                if c.beside == "scan":
                    scan(c)

            dve.memset(ln_ve[:, :], 0.0).then_inc(z_bank_free, 1)
            dve.memset(post_ve[:, :], 0.0).then_inc(z_bank_free, 1)
            for s in range(ST):
                dve.wait_ge(x0_arrived[s], 16)
                ln(s, s % 2, x_tok[:, s, :])
                if s >= 1:
                    split_xt(s - 1, 0, s - 1)
            split_xt(ST - 1, 0, ST - 1)
            dve.wait_ge(exp_done, 1)
            dve.tensor_scalar(lam_tmp[:, 0, :], lam_tmp[:, 1, :], 1.0, None, ALU.add).then_inc(lam_steps, 1)
            dve.wait_ge(lam_steps, 1)
            dve.reciprocal(lam[:, :], lam_tmp[:, 0, :]).then_inc(lam_steps, 1)
            dve.wait_ge(lam_steps, 2)
            dve.wait_ge(rows_arrived, 48)
            walk(dve, step)
            add_y(passes - 1, tiles - 1)

        @block.tensor
        def _(pe):
            def three(dst, a_hi, a_lo, b_hi, b_lo, start, stop):
                pe.matmul(dst, a_hi, b_hi, start=start, stop=False)
                pe.matmul(dst, a_hi, b_lo, start=False, stop=False)
                return pe.matmul(dst, a_lo, b_hi, start=False, stop=stop)

            def turn(f, sp):
                pe.wait_ge(row_ready, f + 1)
                wait(pe, xt_lo_ready, f)
                for c in range(DT):
                    last = pe.transpose(aux_ps[1][:, c * P:(c + 1) * P], rows[:, sp, c * P:(c + 1) * P],
                                        ident[:, :])
                last.then_inc(turned, 1)

            def down(slot, g, start, stop):
                pe.wait_ge(hid_lo_ready, g + 1)
                pe.wait_ge(dn_lo_ready, g + 1)
                for q in range(ST):
                    a = slice(q * P, (q + 1) * P)
                    last = three(down_ps[q][:, :], hid_hi[:, slot, a], hid_lo[:, slot, a], dn_hi[:, slot, :],
                                 dn_lo[:, slot, :], start, stop)
                last.then_inc(down_done, 1)

            def step(c):
                g = c.p * HT + c.t
                at = c.t if isinstance(c.t, int) else None
                if c.beside == "post":
                    pe.wait_ge(scan_sum_ready, (c.tile + 1) * DT)
                    wait(pe, post_steps, (c.tile * ST + c.s) * 3)
                    for e in range(DT):
                        last = pe.transpose(aux_ps[0][:, e * P:(e + 1) * P],
                                            scan_sum[:, e, c.s * P:(c.s + 1) * P], ident[:, :])
                    last.then_inc(turned_back, 1)
                if at == 0:
                    pe.wait_ge(xt_lo_ready, c.f0)
                for base, dst, free, done in ((0, gate_ps, silu_done, gate_done),
                                              (DT * P, up_ps, hid_done, up_done)):
                    pe.wait_ge(gu_lo_ready, g + 1)
                    wait(pe, free, g)
                    for k in range(DT):
                        a = slice(base + k * P, base + (k + 1) * P)
                        last = three(dst[:, :], gu_hi[:, c.tp, a], gu_lo[:, c.tp, a], xt_hi[:, c.odd, k, :],
                                     xt_lo[:, c.odd, k, :], k == 0, k == DT - 1)
                    last.then_inc(done, 1)
                if c.beside in ("ln", "pre"):
                    turn(c.f, c.sp)
                if at == 0:
                    if c.done is not None:
                        down((c.tp + 1) % 2, g - 1, False, True)
                else:
                    if at == 1:
                        wait(pe, y_added, c.p * ST)
                    down((c.tp + 1) % 2, g - 1, at == 1, False)
                if c.beside == "post":
                    turn(c.f, c.sp)
                if c.beside == "scan":
                    unit = c.tile * DT + c.s
                    if c.sp == 0:
                        pe.wait_ge(xt_lo_ready, c.f0 + ST)
                    pe.wait_ge(w_scan_lo_ready, unit + 1)
                    pe.wait_ge(z_bank_free, unit + 1)
                    for k in range(DT):
                        a = slice(k * P, (k + 1) * P)
                        last = three(aux_ps[c.sp][:, :], w_scan_hi[:, a], w_scan_lo[:, a],
                                     xt_hi[:, 1 - c.odd, k, :], xt_lo[:, 1 - c.odd, k, :], k == 0, k == DT - 1)
                    last.then_inc(z_done, 1)

            pe.wait_ge(ident_ready, 1)
            for f in range(ST):
                turn(f, f % 2)
            walk(pe, step, unroll_post=True)
            down(LAST % 2, passes * HT - 1, False, True)


def kernel(**inputs):
    import numpy as np
    import concourse.bacc as bacc
    from concourse.bass_utils import run_bass_kernel_spmd

    def tiles_of(w):
        r, f = w.shape
        return w.reshape(r // P, P, f // P, P).transpose(0, 3, 2, 1)

    x = np.ascontiguousarray(inputs["L0_attn_x"])
    gate = tiles_of(np.asarray(inputs["L0_ffn_w_gate"]))
    up = tiles_of(np.asarray(inputs["L0_ffn_w_up"]))
    down = np.asarray(inputs["L0_ffn_w_down"])
    n = gate.shape[0]
    w_ffn = np.concatenate([gate.reshape(n, P, -1), up.reshape(n, P, -1), down.T.reshape(n, P, -1)], axis=2)
    w_scan = tiles_of(np.asarray(inputs["L0_attn_W"]))
    arrays = {
        "x_in": x,
        "w_ffn_in": np.ascontiguousarray(w_ffn),
        "w_scan_in": np.ascontiguousarray(w_scan.reshape(w_scan.shape[0], P, -1)),
        "lam_logit_in": np.ascontiguousarray(inputs["L0_attn_lam_logit"]),
        "eta_in": np.ascontiguousarray(inputs["L0_attn_eta"]),
        "gamma_in": np.ascontiguousarray(inputs["L0_attn_gamma"]),
        "beta_in": np.ascontiguousarray(inputs["L0_attn_beta"]),
    }
    nc = bacc.Bacc("TRN2", target_bir_lowering=False, num_devices=1, dynamic_dma_scratch_size=1024)
    args = [nc.dram_tensor(name, a.shape, F32, kind="ExternalInput").ap() for name, a in arrays.items()]
    out = nc.dram_tensor("out", x.shape, F32, kind="ExternalOutput").ap()
    macaron_kernel(nc, *args, out)
    r = run_bass_kernel_spmd(nc, [arrays], core_ids=[0])
    return r.results[0]["out"]
```

```python
from collections import namedtuple
from contextlib import ExitStack

import concourse.bass as bass
from concourse import mybir

F32 = mybir.dt.float32
F32R = mybir.dt.float32r
ALU = mybir.AluOpType
ACT = mybir.ActivationFunctionType

P = 128
EPS = 1e-5

Step = namedtuple("Step", "p odd t tp beside s sp tile f0 f done last")


def macaron_kernel(nc, x_in, w_ffn_in, w_scan_in, lam_logit_in, eta_in, gamma_in, beta_in, out):
    tiles, tokens, D = x_in.shape
    H = w_ffn_in.shape[0] * P
    K = lam_logit_in.shape[0]
    DT = D // P
    ST = tokens // P
    HT = H // P
    GU = 2 * DT * P
    LAST = HT - 1
    passes = 2 * tiles
    PRE, SCAN, POST = 2, 6, 11
    WARM = 24
    SQ = 32
    assert tokens == 512 and D == 512 and DT == ST == 4 and HT == 16 and tiles == 4 and K == 4

    with ExitStack() as ctx:
        def sb(name, shape, dt=F32):
            return ctx.enter_context(nc.sbuf_tensor(name, shape, dt))

        def sem(name):
            return ctx.enter_context(nc.semaphore(name))

        w_ffn = sb("w_ffn", [P, HT, GU + D])
        w_scan = sb("w_scan", [P, DT * P])
        w_scan_hi = sb("w_scan_hi", [P, DT * P], F32R)
        w_scan_lo = sb("w_scan_lo", [P, DT * P], F32R)
        gu_hi = sb("gu_hi", [P, 2, GU], F32R)
        gu_lo = sb("gu_lo", [P, 2, GU], F32R)
        dn_hi = sb("dn_hi", [P, 2, D], F32R)
        dn_lo = sb("dn_lo", [P, 2, D], F32R)
        xt_hi = sb("xt_hi", [P, 2, DT, tokens], F32R)
        xt_lo = sb("xt_lo", [P, 2, DT, tokens], F32R)
        hid = sb("hid", [P, 2, tokens])
        hid_hi = sb("hid_hi", [P, 2, tokens], F32R)
        hid_lo = sb("hid_lo", [P, 2, tokens], F32R)
        x_tok = sb("x_tok", [P, tiles * ST, D])
        rows = sb("rows", [P, 2, D])
        row_t = sb("row_t", [P, DT, P])
        scan_sum = sb("scan_sum", [P, DT, tokens])
        gamma = sb("gamma", [P, D])
        beta = sb("beta", [P, D])
        ident = sb("ident", [P, P])
        lam = sb("lam", [P, K])
        lam_tmp = sb("lam_tmp", [P, 2, K])
        eta = sb("eta", [P, K])
        minus_half = sb("minus_half", [P, ST])
        ln_stats = sb("ln_stats", [P, ST, 6])
        ln_mv = sb("ln_mv", [P, ST, 2])
        ln_ve = sb("ln_ve", [P, ST])
        ln_rstd = sb("ln_rstd", [P, ST])
        post_stats = sb("post_stats", [P, 6])
        post_mv = sb("post_mv", [P, 2])
        post_ve = sb("post_ve", [P, 1])
        post_rstd = sb("post_rstd", [P, 1])

        def bank(name):
            return ctx.enter_context(nc.psum_tensor(name, [P, 512], F32))

        gate_ps = bank("gate_ps")
        up_ps = bank("up_ps")
        down_ps = [bank(f"down_ps{q}") for q in range(ST)]
        aux_ps = [bank(f"aux_ps{q}") for q in range(2)]

        def by_tile(ps):
            return ps[:, :].rearrange("p (c n) -> p c n", c=DT)

        w_arrived = [sem(f"w_arrived{t}") for t in range(HT)]
        gate0_arrived = sem("gate0_arrived")
        gate0_hi_ready = sem("gate0_hi_ready")
        gate0_lo_ready = sem("gate0_lo_ready")
        last_down_done = sem("last_down_done")
        x0_arrived = [sem(f"x0_arrived{s}") for s in range(ST)]
        x_arrived = [sem(f"x_arrived{b}") for b in range(tiles)]
        lam_arrived = sem("lam_arrived")
        rows_arrived = sem("rows_arrived")
        w_scan_arrived = sem("w_scan_arrived")
        stored = sem("stored")
        ident_zero = sem("ident_zero")
        ident_ready = sem("ident_ready")
        exp_done = sem("exp_done")
        lam_steps = sem("lam_steps")
        gu_hi_ready = sem("gu_hi_ready")
        gu_lo_ready = sem("gu_lo_ready")
        dn_hi_ready = sem("dn_hi_ready")
        dn_lo_ready = sem("dn_lo_ready")
        gate_done = sem("gate_done")
        up_done = sem("up_done")
        down_done = sem("down_done")
        silu_done = sem("silu_done")
        hid_done = sem("hid_done")
        hid_hi_ready = sem("hid_hi_ready")
        hid_lo_ready = sem("hid_lo_ready")
        y_added = sem("y_added")
        ln_mv_done = sem("ln_mv_done")
        ln_ve_done = sem("ln_ve_done")
        ln_rstd_done = sem("ln_rstd_done")
        row_ready = sem("row_ready")
        turned = sem("turned")
        xt_hi_ready = sem("xt_hi_ready")
        xt_lo_ready = sem("xt_lo_ready")
        w_scan_hi_ready = sem("w_scan_hi_ready")
        w_scan_lo_ready = sem("w_scan_lo_ready")
        z_done = sem("z_done")
        z_bank_free = sem("z_bank_free")
        scan_steps = sem("scan_steps")
        scan_sum_ready = sem("scan_sum_ready")
        turned_back = sem("turned_back")
        post_mv_done = sem("post_mv_done")
        post_ve_done = sem("post_ve_done")
        post_rstd_done = sem("post_rstd_done")
        post_steps = sem("post_steps")

        def wait(eng, semaphore, n):
            if isinstance(n, int) and n <= 0:
                return
            eng.wait_ge(semaphore, n)

        def ln_count(f):
            return f - ST + 2

        def walk(eng, step, unroll_first=False, unroll_post=False):
            def run(t, count, beside, p, odd, tile, f, done, last=False, unroll=False):
                def pair(t, s, tp, n):
                    for u in range(n):
                        step(Step(p, odd, t + u, (tp + u) % 2, beside, s + u, u % 2, tile, f,
                                  f + s + u, done, last))
                if count <= 2 or unroll:
                    for s in range(0, count, 2):
                        pair(t + s, s, t % 2, min(2, count - s))
                else:
                    with eng.Fori(0, count // 2) as k:
                        pair(2 * k + t, 2 * k, t % 2, 2)

            def one_pass(p, odd, kind, tile, f, done, final=False):
                plain = dict(p=p, odd=odd, tile=tile, f=f, done=done)
                first = dict(plain, unroll=unroll_first and isinstance(p, int) and p == 0)
                if kind == "scan":
                    run(0, PRE, "", **first)
                    run(PRE, ST, "pre", **plain)
                    run(SCAN, DT, "scan", **plain)
                    run(SCAN + DT, POST - SCAN - DT, "", **plain)
                    run(POST, ST, "post", p, odd, tile, f + ST, done, unroll=unroll_post)
                    run(LAST, 1, "", last=final, **plain)
                else:
                    run(0, PRE, "", **first)
                    if kind == "ln":
                        run(PRE, ST, "ln", **first)
                        run(PRE + ST, LAST - 1 - PRE - ST, "", **first)
                    else:
                        run(PRE, LAST - 1 - PRE, "", **first)
                    run(LAST - 1, 1, "", **plain)
                    run(LAST, 1, "", last=final, **plain)

            one_pass(0, 0, "ln", 1, ST, None)
            one_pass(1, 1, "scan", 0, 2 * ST, 0)
            with eng.Fori(1, tiles - 1) as i:
                one_pass(2 * i, 0, "ln", i + 1, 12 * i + 4, i)
                one_pass(2 * i + 1, 1, "scan", i, 12 * i + 8, i - 1)
            one_pass(passes - 2, 0, "scan", tiles - 1, 12 * (tiles - 1) + 4, tiles - 1)
            one_pass(passes - 1, 1, "", None, 12 * tiles, tiles - 2, final=True)

        block = ctx.enter_context(nc.Block())

        @block.sync
        def _(sp):
            x_v = x_in.rearrange("b (s p) d -> b p s d", p=P)
            out_v = out.rearrange("b (s p) d -> b p s d", p=P)

            def load_w(t):
                sp.dma_start(w_ffn[:, t, :], w_ffn_in[t]).then_inc(w_arrived[t], 16)

            def load_x(b):
                sp.dma_start(x_tok[:, b * ST:(b + 1) * ST, :], x_v[b]).then_inc(x_arrived[b], 16)

            def load_w_scan(tile, j):
                wait(sp, w_scan_lo_ready, tile * DT + j)
                sp.dma_start(w_scan[:, :], w_scan_in[j]).then_inc(w_scan_arrived, 16)

            def store(b, p):
                sp.wait_ge(y_added, (p + 1) * ST)
                sp.dma_start(out_v[b], x_tok[:, bass.ds(b * ST, ST), :]).then_inc(stored, 16)

            for s in range(ST):
                sp.dma_start(x_tok[:, s, :], x_v[0, :, s, :]).then_inc(x0_arrived[s], 16)
            sp.dma_start(w_ffn[:, 0, 0:DT * P], w_ffn_in[0, :, 0:DT * P]).then_inc(gate0_arrived, 16)
            sp.dma_start(w_ffn[:, 0, DT * P:GU + D], w_ffn_in[0, :, DT * P:GU + D]).then_inc(w_arrived[0], 16)
            load_w(1)
            load_w(2)
            load_x(1)
            for t in range(3, HT):
                load_w(t)
            for row, row_in, n in ((eta, eta_in, K), (gamma, gamma_in, D), (beta, beta_in, D)):
                sp.dma_start(row[:, :], row_in.rearrange("(o d) -> o d", o=1).to_broadcast([P, n])
                             ).then_inc(rows_arrived, 16)
            for b in range(2, tiles):
                load_x(b)
            for j in range(DT):
                load_w_scan(0, j)
            with sp.Fori(1, tiles - 1) as i:
                store(i - 1, 2 * i)
                with sp.Fori(0, DT) as j:
                    load_w_scan(i, j)
            for j in range(DT):
                load_w_scan(tiles - 1, j)
            store(tiles - 2, passes - 2)
            for q in range(ST):
                sp.wait_ge(y_added, (passes - 1) * ST + q + 1)
                sp.dma_start(out_v[tiles - 1, :, q, :], x_tok[:, (tiles - 1) * ST + q, :]).then_inc(stored, 16)
            sp.wait_ge(stored, 16 * (tiles - 1 + ST))

        @block.scalar
        def _(act):
            def split_gu(p, t, slot, g):
                if isinstance(p, int) and p == 0:
                    act.wait_ge(w_arrived[t], 16)
                wait(act, up_done, g - 1)
                act.copy(gu_hi[:, slot, :], w_ffn[:, t, 0:GU]).then_inc(gu_hi_ready, 1)

            def split_xt(f, slot, s, xt):
                act.wait_ge(turned, f + 1)
                act.copy(xt_hi[:, slot, :, bass.ds(s * P, P)], xt).then_inc(xt_hi_ready, 1)

            def step(c):
                g = c.p * HT + c.t
                if not c.last:
                    last = isinstance(c.t, int) and c.t == LAST
                    if last:
                        split_gu(c.p + 1, 0, (c.tp + 1) % 2, g + 1)
                    else:
                        split_gu(c.p, c.t + 1, (c.tp + 1) % 2, g + 1)
                wait(act, down_done, g - 1)
                act.copy(dn_hi[:, c.tp, :], w_ffn[:, c.t, GU:GU + D]).then_inc(dn_hi_ready, 1)
                act.wait_ge(gate_done, g + 1)
                wait(act, hid_lo_ready, g - 1)
                act.activation(hid[:, c.tp, :], gate_ps[:, :], ACT.Silu).then_inc(silu_done, 1)
                if c.beside == "scan":
                    act.wait_ge(w_scan_arrived, (c.tile * DT + c.s) * 16 + 16)
                    act.copy(w_scan_hi[:, :], w_scan[:, :]).then_inc(w_scan_hi_ready, 1)
                act.wait_ge(hid_done, g + 1)
                wait(act, down_done, g - 1)
                act.copy(hid_hi[:, c.tp, :], hid[:, c.tp, :]).then_inc(hid_hi_ready, 1)
                if c.beside in ("ln", "pre", "post"):
                    split_xt(c.f, 1 - c.odd, c.s, row_t[:, :, :] if c.beside != "post" else by_tile(aux_ps[1]))

            act.dma_start(lam_tmp[:, 0, :], lam_logit_in.rearrange("(o k) -> o k", o=1).to_broadcast([P, K])
                          ).then_inc(lam_arrived, 16)
            act.wait_ge(lam_arrived, 16)
            act.activation(lam_tmp[:, 1, :], lam_tmp[:, 0, :], ACT.Exp, scale=-1.0).then_inc(exp_done, 1)
            act.wait_ge(gate0_arrived, 16)
            act.copy(gu_hi[:, 0, 0:DT * P], w_ffn[:, 0, 0:DT * P]).then_inc(gate0_hi_ready, 1)
            for s in range(ST):
                split_xt(s, 0, s, by_tile(down_ps[s]))
            act.wait_ge(w_arrived[0], 16)
            act.copy(gu_hi[:, 0, DT * P:GU], w_ffn[:, 0, DT * P:GU]).then_inc(gu_hi_ready, 1)
            walk(act, step, unroll_first=True)

        @block.gpsimd
        def _(pool):
            def ln(f, u):
                pool.wait_ge(ln_ve_done, ln_count(f))
                pool.tensor_tensor(ln_rstd[:, u:u + 1], ln_ve[:, u:u + 1], minus_half[:, 0:1], ALU.pow
                                   ).then_inc(ln_rstd_done, 1)

            def post_norm(n):
                pool.wait_ge(post_ve_done, n + 1)
                pool.tensor_tensor(post_rstd[:, :], post_ve[:, :], minus_half[:, 0:1], ALU.pow
                                   ).then_inc(post_rstd_done, 1)

            def split_gu(t, slot, g):
                pool.wait_ge(gu_hi_ready, g + 1)
                pool.tensor_tensor(gu_lo[:, slot, :], w_ffn[:, t, 0:GU], gu_hi[:, slot, :].bitcast(F32),
                                   ALU.subtract).then_inc(gu_lo_ready, 1)

            def step(c):
                g = c.p * HT + c.t
                if c.beside in ("ln", "pre"):
                    ln(c.f, c.sp)
                if c.beside == "post":
                    post_norm(c.tile * ST + c.s)
                if not c.last:
                    last = isinstance(c.t, int) and c.t == LAST
                    split_gu(0 if last else c.t + 1, (c.tp + 1) % 2, g + 1)
                if c.beside == "post":
                    ln(c.f, c.sp)
                pool.wait_ge(dn_hi_ready, g + 1)
                pool.tensor_tensor(dn_lo[:, c.tp, :], w_ffn[:, c.t, GU:GU + D], dn_hi[:, c.tp, :].bitcast(F32),
                                   ALU.subtract).then_inc(dn_lo_ready, 1)
                if c.beside == "scan":
                    pool.wait_ge(w_scan_hi_ready, c.tile * DT + c.s + 1)
                    pool.tensor_tensor(w_scan_lo[:, :], w_scan[:, :], w_scan_hi[:, :].bitcast(F32),
                                       ALU.subtract).then_inc(w_scan_lo_ready, 1)

            pool.memset(ident[:, :], 0.0).then_inc(ident_zero, 1)
            pool.memset(minus_half[:, :], -0.5).then_inc(ident_zero, 1)
            pool.wait_ge(ident_zero, 2)
            pool.affine_select(out=ident[:, :], in_=ident[:, :], compare_op=ALU.not_equal, fill=1.0, base=0,
                               pattern=[[-1, P]], channel_multiplier=1).then_inc(ident_ready, 1)
            pool.wait_ge(ln_ve_done, 1)
            pool.tensor_tensor(ln_rstd[:, :], ln_ve[:, :], minus_half[:, :], ALU.pow
                               ).then_inc(ln_rstd_done, 1)
            pool.wait_ge(gate0_hi_ready, 1)
            pool.tensor_tensor(gu_lo[:, 0, 0:DT * P], w_ffn[:, 0, 0:DT * P], gu_hi[:, 0, 0:DT * P].bitcast(F32),
                               ALU.subtract).then_inc(gate0_lo_ready, 1)
            pool.wait_ge(gu_hi_ready, 1)
            pool.tensor_tensor(gu_lo[:, 0, DT * P:GU], w_ffn[:, 0, DT * P:GU],
                               gu_hi[:, 0, DT * P:GU].bitcast(F32), ALU.subtract).then_inc(gu_lo_ready, 1)
            walk(pool, step)

        @block.vector
        def _(dve):
            def stats(f, u, x):
                dve.bn_stats(ln_stats[:, u, :], x)
                dve.drain()
                dve.bn_aggr(ln_mv[:, u, :], ln_stats[:, u, :]).then_inc(ln_mv_done, 1)
                dve.wait_ge(ln_mv_done, f + 1)
                dve.tensor_scalar(ln_ve[:, u:u + 1], ln_mv[:, u, 1:2], EPS, None, ALU.add).then_inc(ln_ve_done, 1)

            def norm(f, u, x, row):
                dve.wait_ge(ln_rstd_done, ln_count(f))
                dve.tensor_scalar(row, x, ln_mv[:, u, 0:1], ln_rstd[:, u:u + 1], ALU.subtract,
                                  ALU.mult).then_inc(row_ready, 1)

            def turn(f):
                dve.wait_ge(row_ready, f + 1)
                dve.transpose(rows[:, 1, :], rows[:, 0, :])
                blocks = rows[:, 1, :].rearrange("p (c n) -> p c n", c=DT)
                dve.drain()
                dve.wait_ge(xt_hi_ready, f)
                for tok in range(0, P, SQ):
                    for feat in range(0, P, SQ):
                        last = dve.tensor_copy(row_t[feat:feat + SQ, :, tok:tok + SQ],
                                               blocks[tok:tok + SQ, :, feat:feat + SQ])
                last.then_inc(turned, 1)

            def split_xt(f, slot, s, xt):
                dve.wait_ge(xt_hi_ready, f + 1)
                dst = bass.ds(s * P, P)
                dve.tensor_tensor(xt_lo[:, slot, :, dst], xt,
                                  xt_hi[:, slot, :, dst].bitcast(F32), ALU.subtract).then_inc(xt_lo_ready, 1)

            def scan(c):
                n = c.tile * DT + c.s
                z = aux_ps[c.sp][:, :]
                total = scan_sum[:, c.s, :]

                def m(k):
                    return dve.tensor_tensor_scan(rows[:, k % 2, :], lam[:, k:k + 1].to_broadcast([P, tokens]),
                                                  z, 0.0, ALU.mult, ALU.add)

                def add(k, to):
                    return dve.scalar_tensor_tensor(total, rows[:, k % 2, :], eta[:, k:k + 1], to, ALU.mult,
                                                    ALU.add)

                dve.wait_ge(rows_arrived, 48)
                dve.drain()
                dve.wait_ge(z_done, n + 1)
                m(0).then_inc(scan_steps, 1)
                m(1).then_inc(scan_steps, 1)
                dve.wait_ge(scan_steps, n * 6 + 1)
                add(0, z).then_inc(scan_steps, 1)
                dve.wait_ge(scan_steps, n * 6 + 3)
                m(2).then_inc(scan_steps, 1)
                add(1, total).then_inc(scan_steps, 1)
                dve.wait_ge(scan_steps, n * 6 + 5)
                m(3).then_inc(z_bank_free, 1)
                add(2, total).then_inc(scan_steps, 1)
                dve.wait_ge(z_bank_free, n + 3)
                dve.wait_ge(scan_steps, n * 6 + 6)
                add(3, total).then_inc(scan_sum_ready, 1)

            def post(c):
                n = c.tile * ST + c.s
                x = x_tok[:, c.tile * ST + c.s, :]
                dve.wait_ge(turned_back, n + 1)
                dve.bn_stats(post_stats[:, :], aux_ps[0][:, :])
                dve.drain()
                dve.bn_aggr(post_mv[:, :], post_stats[:, :]).then_inc(post_mv_done, 1)
                dve.wait_ge(post_mv_done, n + 1)
                dve.tensor_scalar(post_ve[:, :], post_mv[:, 1:2], EPS, None, ALU.add).then_inc(post_ve_done, 1)
                dve.wait_ge(turned, c.f - 1)
                dve.scalar_tensor_tensor(rows[:, c.sp, :], aux_ps[0][:, :], post_mv[:, 0:1], gamma[:, :],
                                         ALU.subtract, ALU.mult).then_inc(post_steps, 1)
                dve.wait_ge(post_steps, n * 3 + 1)
                dve.wait_ge(post_rstd_done, n + 1)
                dve.scalar_tensor_tensor(rows[:, c.sp, :], rows[:, c.sp, :], post_rstd[:, 0:1], beta[:, :],
                                         ALU.mult, ALU.add).then_inc(post_steps, 1)
                dve.wait_ge(post_steps, n * 3 + 2)
                dve.tensor_tensor(x, x, rows[:, c.sp, :], ALU.add).then_inc(post_steps, 1)

            def add_y(p, b):
                dve.wait_ge(down_done, (p + 1) * HT)
                for q in range(ST):
                    x = x_tok[:, b * ST + q, :]
                    dve.scalar_tensor_tensor(x, down_ps[q][:, :], 0.5, x, ALU.mult, ALU.add).then_inc(y_added, 1)

            def step(c):
                g = c.p * HT + c.t
                if c.beside == "ln":
                    for b in (1,) if isinstance(c.p, int) and c.p == 0 else range(2, tiles):
                        dve.wait_ge(x_arrived[b], 16)
                if c.beside == "post":
                    post(c)
                if c.beside in ("pre", "post"):
                    dve.drain()
                if c.beside in ("ln", "pre", "post"):
                    x = x_tok[:, c.tile * ST + c.s, :]
                    stats(c.f, c.sp, x)
                    if c.beside == "post":
                        dve.wait_ge(turned, c.f - 1)
                        norm(c.f, c.sp, x, rows[:, c.sp, :])
                    else:
                        dve.wait_ge(turned, c.f)
                        norm(c.f, c.sp, x, rows[:, 0, :])
                        turn(c.f)
                dve.wait_ge(silu_done, g + 1)
                dve.wait_ge(up_done, g + 1)
                dve.tensor_tensor(hid[:, c.tp, :], hid[:, c.tp, :], up_ps[:, :], ALU.mult).then_inc(hid_done, 1)
                dve.wait_ge(hid_hi_ready, g + 1)
                wait(dve, down_done, g - 1)
                dve.tensor_tensor(hid_lo[:, c.tp, :], hid[:, c.tp, :], hid_hi[:, c.tp, :].bitcast(F32),
                                  ALU.subtract).then_inc(hid_lo_ready, 1)
                if isinstance(c.t, int) and c.t == 0 and c.done is not None:
                    add_y(c.p - 1, c.done)
                if c.beside in ("ln", "pre", "post"):
                    split_xt(c.f, 1 - c.odd, c.s, row_t[:, :, :] if c.beside != "post" else by_tile(aux_ps[1]))
                if c.beside == "scan":
                    scan(c)

            dve.memset(post_mv[:, :], 0.0).then_inc(z_bank_free, 1)
            dve.memset(post_ve[:, :], 0.0).then_inc(z_bank_free, 1)
            for s in range(ST):
                dve.wait_ge(x0_arrived[s], 16)
                dve.bn_stats(ln_stats[:, s, :], x_tok[:, s, :])
            dve.drain()
            for s in range(ST):
                dve.bn_aggr(ln_mv[:, s, :], ln_stats[:, s, :]).then_inc(ln_mv_done, 1)
            dve.wait_ge(ln_mv_done, ST)
            dve.tensor_scalar(ln_ve[:, :], ln_mv[:, :, 1], EPS, None, ALU.add).then_inc(ln_ve_done, 1)
            dve.wait_ge(ln_rstd_done, 1)
            for s in range(ST):
                dve.tensor_scalar(scan_sum[:, s, :], x_tok[:, s, :], ln_mv[:, s, 0:1], ln_rstd[:, s:s + 1],
                                  ALU.subtract, ALU.mult).then_inc(row_ready, 1)
            for s in range(ST):
                split_xt(s, 0, s, by_tile(down_ps[s]))
            dve.wait_ge(exp_done, 1)
            dve.tensor_scalar(lam_tmp[:, 0, :], lam_tmp[:, 1, :], 1.0, None, ALU.add).then_inc(lam_steps, 1)
            dve.wait_ge(lam_steps, 1)
            dve.reciprocal(lam[:, :], lam_tmp[:, 0, :]).then_inc(lam_steps, 1)
            dve.wait_ge(lam_steps, 2)
            walk(dve, step)
            for q in range(ST):
                x = x_tok[:, (tiles - 1) * ST + q, :]
                dve.wait_ge(last_down_done, q + 1)
                dve.scalar_tensor_tensor(x, down_ps[q][:, :], 0.5, x, ALU.mult, ALU.add).then_inc(y_added, 1)

        @block.tensor
        def _(pe):
            def three(dst, a_hi, a_lo, b_hi, b_lo, start, stop):
                pe.matmul(dst, a_hi, b_hi, start=start, stop=False)
                pe.matmul(dst, a_hi, b_lo, start=False, stop=False)
                return pe.matmul(dst, a_lo, b_hi, start=False, stop=stop)

            def turn(f, row, ps):
                pe.wait_ge(row_ready, f + 1)
                for c in range(DT):
                    last = pe.transpose(ps[:, c * P:(c + 1) * P], row[:, c * P:(c + 1) * P], ident[:, :])
                last.then_inc(turned, 1)

            def down(slot, g, start, stop, final=False):
                pe.wait_ge(hid_lo_ready, g + 1)
                pe.wait_ge(dn_lo_ready, g + 1)
                for q in range(ST):
                    a = slice(q * P, (q + 1) * P)
                    last = three(down_ps[q][:, :], hid_hi[:, slot, a], hid_lo[:, slot, a], dn_hi[:, slot, :],
                                 dn_lo[:, slot, :], start, stop)
                    if final:
                        last.then_inc(last_down_done, 1)
                if not final:
                    last.then_inc(down_done, 1)

            def step(c):
                g = c.p * HT + c.t
                at = c.t if isinstance(c.t, int) else None
                if c.beside == "post":
                    pe.wait_ge(scan_sum_ready, (c.tile + 1) * DT)
                    wait(pe, post_steps, (c.tile * ST + c.s) * 3)
                    for e in range(DT):
                        last = pe.transpose(aux_ps[0][:, e * P:(e + 1) * P],
                                            scan_sum[:, e, c.s * P:(c.s + 1) * P], ident[:, :])
                    last.then_inc(turned_back, 1)
                if at == 0:
                    pe.wait_ge(xt_hi_ready, c.f0)
                for base, dst, free, done in ((0, gate_ps, silu_done, gate_done),
                                              (DT * P, up_ps, hid_done, up_done)):
                    if at == 0 and isinstance(c.p, int) and c.p == 0 and dst is gate_ps:
                        pe.wait_ge(gate0_lo_ready, 1)
                    else:
                        pe.wait_ge(gu_lo_ready, g + 1)
                    wait(pe, free, g)
                    w = [slice(base + k * P, base + (k + 1) * P) for k in range(DT)]
                    if at == 0 and dst is gate_ps:
                        for k in range(DT):
                            pe.matmul(dst[:, :], gu_hi[:, c.tp, w[k]], xt_hi[:, c.odd, k, :], start=k == 0,
                                      stop=False)
                            pe.matmul(dst[:, :], gu_lo[:, c.tp, w[k]], xt_hi[:, c.odd, k, :], start=False,
                                      stop=False)
                        pe.wait_ge(xt_lo_ready, c.f0)
                        for k in range(DT):
                            last = pe.matmul(dst[:, :], gu_hi[:, c.tp, w[k]], xt_lo[:, c.odd, k, :],
                                             start=False, stop=k == DT - 1)
                    else:
                        for k in range(DT):
                            last = three(dst[:, :], gu_hi[:, c.tp, w[k]], gu_lo[:, c.tp, w[k]],
                                         xt_hi[:, c.odd, k, :], xt_lo[:, c.odd, k, :], k == 0, k == DT - 1)
                    last.then_inc(done, 1)
                if at == 0:
                    if c.done is not None:
                        down((c.tp + 1) % 2, g - 1, False, True)
                else:
                    if at == 1:
                        wait(pe, y_added, c.p * ST)
                    down((c.tp + 1) % 2, g - 1, at == 1, False)
                if c.beside == "post":
                    pe.wait_ge(xt_lo_ready, c.f)
                    turn(c.f, rows[:, c.sp, :], aux_ps[1])
                if c.beside == "scan":
                    unit = c.tile * DT + c.s
                    if c.sp == 0:
                        pe.wait_ge(xt_lo_ready, c.f0 + ST)
                    pe.wait_ge(w_scan_lo_ready, unit + 1)
                    pe.wait_ge(z_bank_free, unit + 1)
                    for k in range(DT):
                        a = slice(k * P, (k + 1) * P)
                        last = three(aux_ps[c.sp][:, :], w_scan_hi[:, a], w_scan_lo[:, a],
                                     xt_hi[:, 1 - c.odd, k, :], xt_lo[:, 1 - c.odd, k, :], k == 0, k == DT - 1)
                    last.then_inc(z_done, 1)

            pe.wait_ge(ident_ready, 1)
            for _ in range(WARM):
                pe.matmul(gate_ps[:, 0:P], ident[:, :], ident[:, :], start=True, stop=True)
            for f in range(ST):
                turn(f, scan_sum[:, f, :], down_ps[f])
            walk(pe, step, unroll_post=True)
            down(LAST % 2, passes * HT - 1, False, True, final=True)


def kernel(**inputs):
    import numpy as np
    import concourse.bacc as bacc
    from concourse.bass_utils import run_bass_kernel_spmd

    def tiles_of(w):
        r, f = w.shape
        return w.reshape(r // P, P, f // P, P).transpose(0, 3, 2, 1)

    x = np.ascontiguousarray(inputs["L0_attn_x"])
    gate = tiles_of(np.asarray(inputs["L0_ffn_w_gate"]))
    up = tiles_of(np.asarray(inputs["L0_ffn_w_up"]))
    down = np.asarray(inputs["L0_ffn_w_down"])
    n = gate.shape[0]
    w_ffn = np.concatenate([gate.reshape(n, P, -1), up.reshape(n, P, -1), down.T.reshape(n, P, -1)], axis=2)
    w_scan = tiles_of(np.asarray(inputs["L0_attn_W"]))
    arrays = {
        "x_in": x,
        "w_ffn_in": np.ascontiguousarray(w_ffn),
        "w_scan_in": np.ascontiguousarray(w_scan.reshape(w_scan.shape[0], P, -1)),
        "lam_logit_in": np.ascontiguousarray(inputs["L0_attn_lam_logit"]),
        "eta_in": np.ascontiguousarray(inputs["L0_attn_eta"]),
        "gamma_in": np.ascontiguousarray(inputs["L0_attn_gamma"]),
        "beta_in": np.ascontiguousarray(inputs["L0_attn_beta"]),
    }
    nc = bacc.Bacc("TRN2", target_bir_lowering=False, num_devices=1, dynamic_dma_scratch_size=1024)
    args = [nc.dram_tensor(name, a.shape, F32, kind="ExternalInput").ap() for name, a in arrays.items()]
    out = nc.dram_tensor("out", x.shape, F32, kind="ExternalOutput").ap()
    macaron_kernel(nc, *args, out)
    r = run_bass_kernel_spmd(nc, [arrays], core_ids=[0])
    return r.results[0]["out"]
```

```python
from collections import namedtuple
from contextlib import ExitStack

import concourse.bass as bass
from concourse import mybir

F32 = mybir.dt.float32
F32R = mybir.dt.float32r
ALU = mybir.AluOpType
ACT = mybir.ActivationFunctionType

P = 128
EPS = 1e-5

Step = namedtuple("Step", "p odd t tp beside s sp tile f0 f done last")


def macaron_kernel(nc, x_in, w_ffn_in, w_scan_in, lam_logit_in, eta_in, gamma_in, beta_in, out):
    tiles, tokens, D = x_in.shape
    H = w_ffn_in.shape[0] * P
    K = lam_logit_in.shape[0]
    DT = D // P
    ST = tokens // P
    HT = H // P
    GU = 2 * DT * P
    LAST = HT - 1
    passes = 2 * tiles
    PRE = 2
    SCAN = PRE + ST
    POST = SCAN + DT + 1
    WARM = 16
    SQ = 32
    assert tokens == 512 and D == 512 and DT == ST == 4 and HT == 16 and tiles == 4 and K == 4

    with ExitStack() as ctx:
        def sb(name, shape, dt=F32):
            return ctx.enter_context(nc.sbuf_tensor(name, shape, dt))

        def sem(name):
            return ctx.enter_context(nc.semaphore(name))

        w_ffn = sb("w_ffn", [P, HT, GU + D])
        w_scan = sb("w_scan", [P, DT * P])
        w_scan_hi = sb("w_scan_hi", [P, DT * P], F32R)
        w_scan_lo = sb("w_scan_lo", [P, DT * P], F32R)
        gu_hi = sb("gu_hi", [P, 2, GU], F32R)
        gu_lo = sb("gu_lo", [P, 2, GU], F32R)
        dn_hi = sb("dn_hi", [P, 2, D], F32R)
        dn_lo = sb("dn_lo", [P, 2, D], F32R)
        xt_hi = sb("xt_hi", [P, 2, DT, tokens], F32R)
        xt_lo = sb("xt_lo", [P, 2, DT, tokens], F32R)
        hid = sb("hid", [P, 2, tokens])
        hid_hi = sb("hid_hi", [P, 2, tokens], F32R)
        hid_lo = sb("hid_lo", [P, 2, tokens], F32R)
        x_tok = sb("x_tok", [P, tiles * ST, D])
        rows = sb("rows", [P, 2, D])
        row_t = sb("row_t", [P, DT, P])
        scan_sum = sb("scan_sum", [P, tokens])
        scan_tok = sb("scan_tok", [P, ST, D])
        gamma = sb("gamma", [P, D])
        beta = sb("beta", [P, D])
        ident = sb("ident", [P, P])
        lam = sb("lam", [P, K])
        lam_tmp = sb("lam_tmp", [P, 2, K])
        eta = sb("eta", [P, K])
        minus_half = sb("minus_half", [P, ST])
        ln_stats = sb("ln_stats", [P, ST, 6])
        ln_mv = sb("ln_mv", [P, ST, 2])
        ln_ve = sb("ln_ve", [P, ST])
        ln_rstd = sb("ln_rstd", [P, ST])
        post_stats = ln_stats[:, 2, :]
        post_mv = ln_mv[:, 2, :]
        post_ve = ln_ve[:, 2:3]
        post_rstd = ln_rstd[:, 2:3]

        def bank(name):
            return ctx.enter_context(nc.psum_tensor(name, [P, 512], F32))

        gate_ps = bank("gate_ps")
        up_ps = bank("up_ps")
        down_ps = [bank(f"down_ps{q}") for q in range(ST)]
        aux_ps = [bank(f"aux_ps{q}") for q in range(2)]

        def by_tile(ps):
            return ps[:, :].rearrange("p (c n) -> p c n", c=DT)

        def place_blocks(copy, parts, blocks, dst, at, placed):
            blocks = blocks.rearrange("p (c n) -> p c n", n=P)
            for a in parts:
                for b in range(0, P, SQ):
                    last = copy(dst[b:b + SQ, :, at + a:at + a + SQ], blocks[a:a + SQ, :, b:b + SQ])
            last.then_inc(placed, 1)

        def parts(eng, c):
            split = P // 4 if c.beside == "post" and c.s < ST else P // 2
            return range(0, split, SQ) if eng is nc.vector else range(split, P, SQ)

        def place_rows(copy, parts):
            place_blocks(copy, parts, rows[:, 1, :], row_t, 0, blocks_placed)

        def place_sum(copy, parts, j):
            place_blocks(copy, parts, row_t[:, :, :].rearrange("p c n -> p (c n)"), scan_tok, j * P,
                         sum_blocks_placed)

        def turns(c):
            if c.beside in ("ln", "pre"):
                return c.f, c.s
            if c.beside == "post" and c.s > 0:
                return c.f - 1, c.s - 1
            return None

        w_arrived = [sem(f"w_arrived{t}") for t in range(HT)]
        gate0_arrived = sem("gate0_arrived")
        gate0_hi_ready = sem("gate0_hi_ready")
        gate0_lo_ready = sem("gate0_lo_ready")
        last_down_done = sem("last_down_done")
        x0_arrived = [sem(f"x0_arrived{s}") for s in range(ST)]
        x_arrived = {b: sem(f"x_arrived{b}") for b in range(1, tiles)}
        lam_arrived = sem("lam_arrived")
        rows_arrived = sem("rows_arrived")
        w_scan_arrived = sem("w_scan_arrived")
        stored = sem("stored")
        ident_zero = sem("ident_zero")
        ident_ready = sem("ident_ready")
        exp_done = sem("exp_done")
        lam_steps = sem("lam_steps")
        gu_hi_ready = sem("gu_hi_ready")
        gu_lo_ready = sem("gu_lo_ready")
        dn_hi_ready = sem("dn_hi_ready")
        dn_lo_ready = sem("dn_lo_ready")
        gate_done = sem("gate_done")
        up_done = sem("up_done")
        down_done = sem("down_done")
        silu_done = sem("silu_done")
        hid_done = sem("hid_done")
        hid_hi_ready = sem("hid_hi_ready")
        hid_lo_ready = sem("hid_lo_ready")
        y_added = sem("y_added")
        ln_mv_done = sem("ln_mv_done")
        ln_ve_done = sem("ln_ve_done")
        ln_rstd_done = sem("ln_rstd_done")
        row_ready = sem("row_ready")
        blocks_turned = sem("blocks_turned")
        blocks_placed = sem("blocks_placed")
        turned = sem("turned")
        xt_hi_ready = sem("xt_hi_ready")
        xt_lo_ready = sem("xt_lo_ready")
        w_scan_hi_ready = sem("w_scan_hi_ready")
        w_scan_lo_ready = sem("w_scan_lo_ready")
        z_done = sem("z_done")
        z_bank_free = sem("z_bank_free")
        scan_steps = sem("scan_steps")
        sum_blocks_turned = sem("sum_blocks_turned")
        sum_blocks_placed = sem("sum_blocks_placed")
        post_mv_done = sem("post_mv_done")
        post_ve_done = sem("post_ve_done")
        post_rstd_done = sem("post_rstd_done")
        post_steps = sem("post_steps")

        def wait(eng, semaphore, n):
            if isinstance(n, int) and n <= 0:
                return
            eng.wait_ge(semaphore, n)

        def ln_count(f):
            return f - ST + 3

        def walk(eng, step, unroll_first=False):
            def run(t, count, beside, p, odd, tile, f, done, last=False, unroll=False):
                def pair(t, s, tp, n):
                    for u in range(n):
                        step(Step(p, odd, t + u, (tp + u) % 2, beside, s + u, u % 2, tile, f,
                                  f + s + u, done, last))
                if count <= 2 or unroll:
                    for s in range(0, count, 2):
                        pair(t + s, s, t % 2, min(2, count - s))
                else:
                    with eng.Fori(0, count // 2) as k:
                        pair(2 * k + t, 2 * k, t % 2, 2)

            def one_pass(p, odd, kind, tile, f, done, final=False):
                plain = dict(p=p, odd=odd, tile=tile, f=f, done=done)
                first = dict(plain, unroll=unroll_first and isinstance(p, int) and p == 0)
                if kind == "scan":
                    run(0, PRE, "", **first)
                    run(PRE, ST, "pre", **plain)
                    for s in range(DT + 1):
                        step(Step(p, odd, SCAN + s, (SCAN + s) % 2, "scan", s, s % 2, tile, f, f + s,
                                  done, False))
                    for s in range(ST + 1):
                        step(Step(p, odd, POST + s, (POST + s) % 2, "post", s, s % 2, tile, f + ST,
                                  f + ST + s, done, False))
                else:
                    run(0, PRE, "", **first)
                    if kind == "ln":
                        run(PRE, ST, "ln", **first)
                        run(PRE + ST, LAST - 1 - PRE - ST, "", **first)
                    else:
                        run(PRE, LAST - 1 - PRE, "", **first)
                    run(LAST - 1, 1, "", **plain)
                    run(LAST, 1, "", last=final, **plain)

            one_pass(0, 0, "ln", 1, ST, None)
            one_pass(1, 1, "scan", 0, 2 * ST, 0)
            with eng.Fori(1, tiles - 1) as i:
                one_pass(2 * i, 0, "ln", i + 1, 12 * i + 4, i)
                one_pass(2 * i + 1, 1, "scan", i, 12 * i + 8, i - 1)
            one_pass(passes - 2, 0, "scan", tiles - 1, 12 * (tiles - 1) + 4, tiles - 1)
            one_pass(passes - 1, 1, "", None, 12 * tiles, tiles - 2, final=True)

        block = ctx.enter_context(nc.Block())

        @block.sync
        def _(sp):
            x_v = x_in.rearrange("b (s p) d -> b p s d", p=P)
            out_v = out.rearrange("b (s p) d -> b p s d", p=P)

            def load_w(t):
                sp.dma_start(w_ffn[:, t, :], w_ffn_in[t]).then_inc(w_arrived[t], 16)

            def load_x(b):
                sp.dma_start(x_tok[:, b * ST:(b + 1) * ST, :], x_v[b]).then_inc(x_arrived[b], 16)

            def load_w_scan(tile, j):
                wait(sp, w_scan_lo_ready, tile * DT + j)
                sp.dma_start(w_scan[:, :], w_scan_in[j]).then_inc(w_scan_arrived, 16)

            def store(b, p):
                sp.wait_ge(y_added, (p + 1) * ST)
                sp.dma_start(out_v[b], x_tok[:, bass.ds(b * ST, ST), :]).then_inc(stored, 16)

            for s in range(ST):
                sp.dma_start(x_tok[:, s, :], x_v[0, :, s, :]).then_inc(x0_arrived[s], 16)
            sp.dma_start(w_ffn[:, 0, 0:DT * P], w_ffn_in[0, :, 0:DT * P]).then_inc(gate0_arrived, 16)
            sp.dma_start(w_ffn[:, 0, DT * P:GU + D], w_ffn_in[0, :, DT * P:GU + D]).then_inc(w_arrived[0], 16)
            load_w(1)
            load_w(2)
            load_x(1)
            for t in range(3, HT):
                load_w(t)
            for row, row_in, n in ((eta, eta_in, K), (gamma, gamma_in, D), (beta, beta_in, D)):
                sp.dma_start(row[:, :], row_in.rearrange("(o d) -> o d", o=1).to_broadcast([P, n])
                             ).then_inc(rows_arrived, 16)
            for b in range(2, tiles):
                load_x(b)
            for j in range(DT):
                load_w_scan(0, j)
            with sp.Fori(1, tiles - 1) as i:
                store(i - 1, 2 * i)
                with sp.Fori(0, DT) as j:
                    load_w_scan(i, j)
            for j in range(DT):
                load_w_scan(tiles - 1, j)
            store(tiles - 2, passes - 2)
            for q in range(ST):
                sp.wait_ge(y_added, (passes - 1) * ST + q + 1)
                sp.dma_start(out_v[tiles - 1, :, q, :], x_tok[:, (tiles - 1) * ST + q, :]).then_inc(stored, 16)
            sp.wait_ge(stored, 16 * (tiles - 1 + ST))

        @block.scalar
        def _(act):
            def split_gu(p, t, slot, g):
                if isinstance(p, int) and p == 0:
                    act.wait_ge(w_arrived[t], 16)
                wait(act, up_done, g - 1)
                act.copy(gu_hi[:, slot, :], w_ffn[:, t, 0:GU]).then_inc(gu_hi_ready, 1)

            def split_first_xt(s):
                act.wait_ge(turned, s + 1)
                act.copy(xt_hi[:, 0, :, s * P:(s + 1) * P], by_tile(down_ps[s])).then_inc(xt_hi_ready, 1)

            def place_part(c):
                if turns(c):
                    act.wait_ge(blocks_turned, turns(c)[0] - ST + 1)
                    place_rows(act.copy, parts(nc.scalar, c))

            def split_xt(c, slot):
                if not turns(c):
                    return
                f, s = turns(c)
                act.wait_ge(blocks_placed, 2 * (f - ST) + 2)
                act.copy(xt_hi[:, slot, :, bass.ds(s * P, P)], row_t[:, :, :]).then_inc(xt_hi_ready, 1)

            def step(c):
                g = c.p * HT + c.t
                if not c.last:
                    last = isinstance(c.t, int) and c.t == LAST
                    if last:
                        split_gu(c.p + 1, 0, (c.tp + 1) % 2, g + 1)
                    else:
                        split_gu(c.p, c.t + 1, (c.tp + 1) % 2, g + 1)
                wait(act, down_done, g - 1)
                act.copy(dn_hi[:, c.tp, :], w_ffn[:, c.t, GU:GU + D]).then_inc(dn_hi_ready, 1)
                if c.beside == "post" and c.s == ST:
                    place_part(c)
                    split_xt(c, 1 - c.odd)
                act.wait_ge(gate_done, g + 1)
                wait(act, hid_lo_ready, g - 1)
                act.activation(hid[:, c.tp, :], gate_ps[:, :], ACT.Silu).then_inc(silu_done, 1)
                if c.beside in ("ln", "pre") or (c.beside == "post" and c.s < ST):
                    place_part(c)
                if c.beside == "post" and c.s < ST:
                    split_xt(c, 1 - c.odd)
                if c.beside == "scan" and c.s < DT:
                    act.wait_ge(w_scan_arrived, (c.tile * DT + c.s) * 16 + 16)
                    act.copy(w_scan_hi[:, :], w_scan[:, :]).then_inc(w_scan_hi_ready, 1)
                if c.beside == "scan" and c.s > 0:
                    act.wait_ge(sum_blocks_turned, c.tile * DT + c.s)
                    place_sum(act.copy, parts(nc.scalar, c), c.s - 1)
                act.wait_ge(hid_done, g + 1)
                wait(act, down_done, g - 1)
                act.copy(hid_hi[:, c.tp, :], hid[:, c.tp, :]).then_inc(hid_hi_ready, 1)
                if c.beside in ("ln", "pre"):
                    split_xt(c, 1 - c.odd)

            act.dma_start(lam_tmp[:, 0, :], lam_logit_in.rearrange("(o k) -> o k", o=1).to_broadcast([P, K])
                          ).then_inc(lam_arrived, 16)
            act.wait_ge(lam_arrived, 16)
            act.activation(lam_tmp[:, 1, :], lam_tmp[:, 0, :], ACT.Exp, scale=-1.0).then_inc(exp_done, 1)
            act.wait_ge(gate0_arrived, 16)
            act.copy(gu_hi[:, 0, 0:DT * P], w_ffn[:, 0, 0:DT * P]).then_inc(gate0_hi_ready, 1)
            act.wait_ge(w_arrived[0], 16)
            act.copy(gu_hi[:, 0, DT * P:GU], w_ffn[:, 0, DT * P:GU]).then_inc(gu_hi_ready, 1)
            for s in range(ST):
                split_first_xt(s)
            walk(act, step, unroll_first=True)

        @block.gpsimd
        def _(pool):
            def ln(f, u):
                pool.wait_ge(ln_ve_done, ln_count(f))
                pool.tensor_tensor(ln_rstd[:, u:u + 1], ln_ve[:, u:u + 1], minus_half[:, 0:1], ALU.pow
                                   ).then_inc(ln_rstd_done, 1)

            def post_norm(n):
                pool.wait_ge(post_ve_done, n + 1)
                pool.tensor_tensor(post_rstd[:, :], post_ve[:, :], minus_half[:, 0:1], ALU.pow
                                   ).then_inc(post_rstd_done, 1)

            def split_gu(t, slot, g):
                pool.wait_ge(gu_hi_ready, g + 1)
                pool.tensor_tensor(gu_lo[:, slot, :], w_ffn[:, t, 0:GU], gu_hi[:, slot, :].bitcast(F32),
                                   ALU.subtract).then_inc(gu_lo_ready, 1)

            def step(c):
                g = c.p * HT + c.t
                if c.beside in ("ln", "pre"):
                    ln(c.f, c.sp)
                if c.beside == "post" and c.s < ST:
                    post_norm(c.tile * ST + c.s)
                if not c.last:
                    last = isinstance(c.t, int) and c.t == LAST
                    split_gu(0 if last else c.t + 1, (c.tp + 1) % 2, g + 1)
                pool.wait_ge(dn_hi_ready, g + 1)
                pool.tensor_tensor(dn_lo[:, c.tp, :], w_ffn[:, c.t, GU:GU + D], dn_hi[:, c.tp, :].bitcast(F32),
                                   ALU.subtract).then_inc(dn_lo_ready, 1)
                if c.beside == "post" and c.s < ST:
                    ln(c.f, c.sp)
                if c.beside == "scan" and c.s < DT:
                    pool.wait_ge(w_scan_hi_ready, c.tile * DT + c.s + 1)
                    pool.tensor_tensor(w_scan_lo[:, :], w_scan[:, :], w_scan_hi[:, :].bitcast(F32),
                                       ALU.subtract).then_inc(w_scan_lo_ready, 1)

            pool.memset(ident[:, :], 0.0).then_inc(ident_zero, 1)
            pool.memset(minus_half[:, :], -0.5).then_inc(ident_zero, 1)
            pool.wait_ge(ident_zero, 2)
            pool.affine_select(out=ident[:, :], in_=ident[:, :], compare_op=ALU.not_equal, fill=1.0, base=0,
                               pattern=[[-1, P]], channel_multiplier=1).then_inc(ident_ready, 1)
            for u in range(0, ST, 2):
                pool.wait_ge(ln_ve_done, u // 2 + 1)
                pool.tensor_tensor(ln_rstd[:, u:u + 2], ln_ve[:, u:u + 2], minus_half[:, u:u + 2], ALU.pow
                                   ).then_inc(ln_rstd_done, 1)
            pool.wait_ge(gate0_hi_ready, 1)
            pool.tensor_tensor(gu_lo[:, 0, 0:DT * P], w_ffn[:, 0, 0:DT * P], gu_hi[:, 0, 0:DT * P].bitcast(F32),
                               ALU.subtract).then_inc(gate0_lo_ready, 1)
            pool.wait_ge(gu_hi_ready, 1)
            pool.tensor_tensor(gu_lo[:, 0, DT * P:GU], w_ffn[:, 0, DT * P:GU],
                               gu_hi[:, 0, DT * P:GU].bitcast(F32), ALU.subtract).then_inc(gu_lo_ready, 1)
            walk(pool, step)

        @block.vector
        def _(dve):
            def stats(f, u, x):
                dve.bn_stats(ln_stats[:, u, :], x)
                dve.drain()
                dve.bn_aggr(ln_mv[:, u, :], ln_stats[:, u, :]).then_inc(ln_mv_done, 1)
                dve.wait_ge(ln_mv_done, f + 1)
                dve.tensor_scalar(ln_ve[:, u:u + 1], ln_mv[:, u, 1:2], EPS, None, ALU.add).then_inc(ln_ve_done, 1)

            def norm(f, u, x, row):
                dve.wait_ge(ln_rstd_done, ln_count(f))
                dve.tensor_scalar(row, x, ln_mv[:, u, 0:1], ln_rstd[:, u:u + 1], ALU.subtract,
                                  ALU.mult).then_inc(row_ready, 1)

            def turn_blocks(f):
                dve.wait_ge(row_ready, f + 1)
                dve.wait_ge(xt_hi_ready, f)
                dve.transpose(rows[:, 1, :], rows[:, 0, :]).then_inc(blocks_turned, 1)
                dve.drain()

            def split_first_xt(s):
                dve.wait_ge(xt_hi_ready, s + 1)
                dst = slice(s * P, (s + 1) * P)
                dve.tensor_tensor(xt_lo[:, 0, :, dst], by_tile(down_ps[s]),
                                  xt_hi[:, 0, :, dst].bitcast(F32), ALU.subtract).then_inc(xt_lo_ready, 1)

            def split_xt(c, slot):
                if not turns(c):
                    return
                f, s = turns(c)
                dve.wait_ge(xt_hi_ready, f + 1)
                dst = bass.ds(s * P, P)
                dve.tensor_tensor(xt_lo[:, slot, :, dst], row_t[:, :, :],
                                  xt_hi[:, slot, :, dst].bitcast(F32), ALU.subtract).then_inc(xt_lo_ready, 1)

            def scan(c):
                n = c.tile * DT + c.s
                z = aux_ps[c.sp][:, :]
                total = scan_sum[:, :]

                def m(k):
                    return dve.tensor_tensor_scan(rows[:, k % 2, :], lam[:, k:k + 1].to_broadcast([P, tokens]),
                                                  z, 0.0, ALU.mult, ALU.add)

                def add(k, to):
                    return dve.scalar_tensor_tensor(total, rows[:, k % 2, :], eta[:, k:k + 1], to, ALU.mult,
                                                    ALU.add)

                dve.wait_ge(rows_arrived, 48)
                dve.wait_ge(z_done, n + 1)
                m(0).then_inc(scan_steps, 1)
                m(1).then_inc(scan_steps, 1)
                dve.wait_ge(scan_steps, n * 6 + 1)
                add(0, z).then_inc(scan_steps, 1)
                dve.wait_ge(scan_steps, n * 6 + 3)
                m(2).then_inc(scan_steps, 1)
                add(1, total).then_inc(scan_steps, 1)
                dve.wait_ge(scan_steps, n * 6 + 5)
                m(3).then_inc(z_bank_free, 1)
                add(2, total).then_inc(scan_steps, 1)
                dve.wait_ge(z_bank_free, n + 1)
                dve.wait_ge(scan_steps, n * 6 + 6)
                add(3, total)
                dve.drain()
                wait(dve, sum_blocks_placed, 2 * n)
                dve.transpose(row_t[:, :, :].rearrange("p c n -> p (c n)"), total).then_inc(sum_blocks_turned, 1)
                dve.drain()
                place_sum(dve.tensor_copy, parts(nc.vector, c), c.s)

            def post(c):
                n = c.tile * ST + c.s
                if c.s < ST:
                    x = x_tok[:, c.tile * ST + c.s, :]
                    dve.wait_ge(sum_blocks_placed, (c.tile + 1) * 2 * DT)
                    dve.bn_stats(post_stats[:, :], scan_tok[:, c.s, :])
                    dve.drain()
                    dve.bn_aggr(post_mv[:, :], post_stats[:, :]).then_inc(post_mv_done, 1)
                    dve.wait_ge(post_mv_done, n + 1)
                    dve.tensor_scalar(post_ve[:, :], post_mv[:, 1:2], EPS, None, ALU.add).then_inc(post_ve_done, 1)
                if c.s > 0:
                    norm(c.f - 1, 1 - c.sp, x_tok[:, c.tile * ST + c.s - 1, :], rows[:, 0, :])
                    turn_blocks(c.f - 1)
                if c.s < ST:
                    dve.scalar_tensor_tensor(rows[:, 0, :], scan_tok[:, c.s, :], post_mv[:, 0:1], gamma[:, :],
                                             ALU.subtract, ALU.mult).then_inc(post_steps, 1)
                if c.s > 0:
                    place_rows(dve.tensor_copy, parts(nc.vector, c))
                if c.s < ST:
                    dve.wait_ge(post_steps, n * 3 + 1)
                    dve.wait_ge(post_rstd_done, n + 1)
                    dve.scalar_tensor_tensor(rows[:, 0, :], rows[:, 0, :], post_rstd[:, 0:1], beta[:, :],
                                             ALU.mult, ALU.add).then_inc(post_steps, 1)
                    dve.wait_ge(post_steps, n * 3 + 2)
                    dve.tensor_tensor(x, x, rows[:, 0, :], ALU.add).then_inc(post_steps, 1)

            def add_y(p, b):
                dve.wait_ge(down_done, (p + 1) * HT)
                for q in range(ST):
                    x = x_tok[:, b * ST + q, :]
                    dve.scalar_tensor_tensor(x, down_ps[q][:, :], 0.5, x, ALU.mult, ALU.add).then_inc(y_added, 1)

            def step(c):
                g = c.p * HT + c.t
                if c.beside == "ln":
                    for b in (1,) if isinstance(c.p, int) and c.p == 0 else range(2, tiles):
                        dve.wait_ge(x_arrived[b], 16)
                if c.beside == "post":
                    post(c)
                if c.beside == "pre":
                    dve.drain()
                if c.beside in ("ln", "pre"):
                    x = x_tok[:, c.tile * ST + c.s, :]
                    stats(c.f, c.sp, x)
                    norm(c.f, c.sp, x, rows[:, 0, :])
                    turn_blocks(c.f)
                    place_rows(dve.tensor_copy, parts(nc.vector, c))
                if c.beside == "post" and c.s == ST:
                    split_xt(c, 1 - c.odd)
                dve.wait_ge(silu_done, g + 1)
                dve.wait_ge(up_done, g + 1)
                dve.tensor_tensor(hid[:, c.tp, :], hid[:, c.tp, :], up_ps[:, :], ALU.mult).then_inc(hid_done, 1)
                if c.beside == "post" and c.s < ST:
                    dve.drain()
                    stats(c.f, c.sp, x_tok[:, c.tile * ST + c.s, :])
                    split_xt(c, 1 - c.odd)
                dve.wait_ge(hid_hi_ready, g + 1)
                wait(dve, down_done, g - 1)
                dve.tensor_tensor(hid_lo[:, c.tp, :], hid[:, c.tp, :], hid_hi[:, c.tp, :].bitcast(F32),
                                  ALU.subtract).then_inc(hid_lo_ready, 1)
                if isinstance(c.t, int) and c.t == 0 and c.done is not None:
                    add_y(c.p - 1, c.done)
                if c.beside in ("ln", "pre"):
                    split_xt(c, 1 - c.odd)
                if c.beside == "scan" and c.s < DT:
                    scan(c)

            def first_stats(u):
                for s in (u, u + 1):
                    dve.wait_ge(x0_arrived[s], 16)
                    dve.bn_stats(ln_stats[:, s, :], x_tok[:, s, :])
                dve.drain()
                for s in (u, u + 1):
                    dve.bn_aggr(ln_mv[:, s, :], ln_stats[:, s, :]).then_inc(ln_mv_done, 1)
                dve.wait_ge(ln_mv_done, u + 2)
                dve.tensor_scalar(ln_ve[:, u:u + 2], ln_mv[:, u:u + 2, 1], EPS, None, ALU.add
                                  ).then_inc(ln_ve_done, 1)

            def first_norm(u):
                dve.wait_ge(ln_rstd_done, u // 2 + 1)
                for s in (u, u + 1):
                    dve.tensor_scalar(scan_tok[:, s, :], x_tok[:, s, :], ln_mv[:, s, 0:1], ln_rstd[:, s:s + 1],
                                      ALU.subtract, ALU.mult).then_inc(row_ready, 1)

            for u in range(0, ST, 2):
                first_stats(u)
            for u in range(0, ST, 2):
                first_norm(u)
            for s in range(ST):
                split_first_xt(s)
            dve.wait_ge(exp_done, 1)
            dve.tensor_scalar(lam_tmp[:, 0, :], lam_tmp[:, 1, :], 1.0, None, ALU.add).then_inc(lam_steps, 1)
            dve.wait_ge(lam_steps, 1)
            dve.reciprocal(lam[:, :], lam_tmp[:, 0, :]).then_inc(lam_steps, 1)
            dve.wait_ge(lam_steps, 2)
            walk(dve, step)
            for q in range(ST):
                x = x_tok[:, (tiles - 1) * ST + q, :]
                dve.wait_ge(last_down_done, q + 1)
                dve.scalar_tensor_tensor(x, down_ps[q][:, :], 0.5, x, ALU.mult, ALU.add).then_inc(y_added, 1)

        @block.tensor
        def _(pe):
            def three(dst, a_hi, a_lo, b_hi, b_lo, start, stop):
                pe.matmul(dst, a_hi, b_hi, start=start, stop=False)
                pe.matmul(dst, a_hi, b_lo, start=False, stop=False)
                return pe.matmul(dst, a_lo, b_hi, start=False, stop=stop)

            def turn(f, row, ps):
                pe.wait_ge(row_ready, f + 1)
                for c in range(DT):
                    last = pe.transpose(ps[:, c * P:(c + 1) * P], row[:, c * P:(c + 1) * P], ident[:, :])
                last.then_inc(turned, 1)

            def down(slot, g, start, stop, final=False):
                pe.wait_ge(hid_lo_ready, g + 1)
                pe.wait_ge(dn_lo_ready, g + 1)
                for q in range(ST):
                    a = slice(q * P, (q + 1) * P)
                    last = three(down_ps[q][:, :], hid_hi[:, slot, a], hid_lo[:, slot, a], dn_hi[:, slot, :],
                                 dn_lo[:, slot, :], start, stop)
                    if final:
                        last.then_inc(last_down_done, 1)
                if not final:
                    last.then_inc(down_done, 1)

            def step(c):
                g = c.p * HT + c.t
                at = c.t if isinstance(c.t, int) else None
                first = at == 0 and isinstance(c.p, int) and c.p == 0
                if at == 0 and not first:
                    pe.wait_ge(xt_hi_ready, c.f0)
                for base, dst, free, done in ((0, gate_ps, silu_done, gate_done),
                                              (DT * P, up_ps, hid_done, up_done)):
                    if first and dst is gate_ps:
                        pe.wait_ge(gate0_lo_ready, 1)
                    else:
                        pe.wait_ge(gu_lo_ready, g + 1)
                    wait(pe, free, g)
                    w = [slice(base + k * P, base + (k + 1) * P) for k in range(DT)]
                    if at == 0 and dst is gate_ps:
                        part = tokens // 2 if first else tokens
                        for a in range(0, tokens, part):
                            cols = slice(a, a + part)
                            if first:
                                pe.wait_ge(xt_hi_ready, (a + part) // P)
                            for k in range(DT):
                                for gu in (gu_hi, gu_lo):
                                    pe.matmul(dst[:, cols], gu[:, c.tp, w[k]], xt_hi[:, c.odd, k, cols],
                                              start=k == 0 and gu is gu_hi, stop=False)
                            pe.wait_ge(xt_lo_ready, (a + part) // P if first else c.f0)
                            for k in range(DT):
                                last = pe.matmul(dst[:, cols], gu_hi[:, c.tp, w[k]], xt_lo[:, c.odd, k, cols],
                                                 start=False, stop=k == DT - 1)
                    else:
                        for k in range(DT):
                            last = three(dst[:, :], gu_hi[:, c.tp, w[k]], gu_lo[:, c.tp, w[k]],
                                         xt_hi[:, c.odd, k, :], xt_lo[:, c.odd, k, :], k == 0, k == DT - 1)
                    last.then_inc(done, 1)
                if at == 0:
                    if c.done is not None:
                        down((c.tp + 1) % 2, g - 1, False, True)
                else:
                    if at == 1:
                        wait(pe, y_added, c.p * ST)
                    down((c.tp + 1) % 2, g - 1, at == 1, False)
                if c.beside == "scan" and c.s < DT:
                    unit = c.tile * DT + c.s
                    if c.sp == 0:
                        pe.wait_ge(xt_lo_ready, c.f0 + ST)
                    pe.wait_ge(w_scan_lo_ready, unit + 1)
                    wait(pe, z_bank_free, unit - 1)
                    for k in range(DT):
                        a = slice(k * P, (k + 1) * P)
                        last = three(aux_ps[c.sp][:, :], w_scan_hi[:, a], w_scan_lo[:, a],
                                     xt_hi[:, 1 - c.odd, k, :], xt_lo[:, 1 - c.odd, k, :], k == 0, k == DT - 1)
                    last.then_inc(z_done, 1)

            pe.wait_ge(ident_ready, 1)
            for _ in range(WARM):
                pe.matmul(gate_ps[:, 0:P], ident[:, :], ident[:, :], start=True, stop=True)
            for f in range(ST):
                turn(f, scan_tok[:, f, :], down_ps[f])
            walk(pe, step)
            down(LAST % 2, passes * HT - 1, False, True, final=True)


def kernel(**inputs):
    import numpy as np
    import concourse.bacc as bacc
    from concourse.bass_utils import run_bass_kernel_spmd

    def tiles_of(w):
        r, f = w.shape
        return w.reshape(r // P, P, f // P, P).transpose(0, 3, 2, 1)

    x = np.ascontiguousarray(inputs["L0_attn_x"])
    gate = tiles_of(np.asarray(inputs["L0_ffn_w_gate"]))
    up = tiles_of(np.asarray(inputs["L0_ffn_w_up"]))
    down = np.asarray(inputs["L0_ffn_w_down"])
    n = gate.shape[0]
    w_ffn = np.concatenate([gate.reshape(n, P, -1), up.reshape(n, P, -1), down.T.reshape(n, P, -1)], axis=2)
    w_scan = tiles_of(np.asarray(inputs["L0_attn_W"]))
    arrays = {
        "x_in": x,
        "w_ffn_in": np.ascontiguousarray(w_ffn),
        "w_scan_in": np.ascontiguousarray(w_scan.reshape(w_scan.shape[0], P, -1)),
        "lam_logit_in": np.ascontiguousarray(inputs["L0_attn_lam_logit"]),
        "eta_in": np.ascontiguousarray(inputs["L0_attn_eta"]),
        "gamma_in": np.ascontiguousarray(inputs["L0_attn_gamma"]),
        "beta_in": np.ascontiguousarray(inputs["L0_attn_beta"]),
    }
    nc = bacc.Bacc("TRN2", target_bir_lowering=False, num_devices=1, dynamic_dma_scratch_size=1024)
    args = [nc.dram_tensor(name, a.shape, F32, kind="ExternalInput").ap() for name, a in arrays.items()]
    out = nc.dram_tensor("out", x.shape, F32, kind="ExternalOutput").ap()
    macaron_kernel(nc, *args, out)
    r = run_bass_kernel_spmd(nc, [arrays], core_ids=[0])
    return r.results[0]["out"]
```
